# Optimizing a Trainium2 kernel written in Bass

```python
import numpy as np
import jax
import jax.numpy as jnp

def _softmax(x, axis=-1):
    return jax.nn.softmax(x, axis=axis)

def _gelu(x):
    return jax.nn.gelu(x, approximate=True)

def _silu(x):
    return jax.nn.silu(x)

def _sigmoid(x):
    return jax.nn.sigmoid(x)

def _layernorm(x, axis=-1, eps=1e-05):
    m = jnp.mean(x, axis=axis, keepdims=True)
    v = jnp.var(x, axis=axis, keepdims=True)
    return (x - m) / jnp.sqrt(v + eps)

def _scatter_add(tgt, idx, src, axis=0):
    return tgt.at[idx].add(src)

def _segment_sum(src, seg, n):
    return jax.ops.segment_sum(src, seg, n)
kernel_name = 'mk_cond_resid_d1_seqx_r8_9592f3'

def setup_inputs(seed: int=0):
    np.random.seed(seed)
    _w = jnp.asarray

    def _rec_inputs():
        import jax
        import jax.numpy as jnp
        _rk = jax.random.key(seed)
        x = -0.000125 + 0.9999 * jax.random.normal(jax.random.fold_in(_rk, 1), (64, 32, 512), jnp.float32)
        _lenS = 32 - jax.random.randint(jax.random.fold_in(_rk, 7), (64,), 0, max(1, 32 // 4) + 1, jnp.int32)
        _lenS2 = 32 - jax.random.randint(jax.random.fold_in(_rk, 8), (64,), 0, max(1, 32 // 4) + 1, jnp.int32)
        itok_B_0_7 = jax.random.randint(jax.random.fold_in(_rk, 11), (64,), 0, 8, jnp.int32)
        return (x, itok_B_0_7)
    x, itok_B_0_7 = _rec_inputs()

    def _L0_cond_setup():
        import jax, jax.numpy as jnp
        import numpy as np
        TOP_K = 2
        LANG_BIAS = 5.0
        SCALING = 32.0 / 16.0
        LANGUAGE_PAD_ID = -1
        key = jax.random.key(seed)
        ks = jax.random.split(key, 6)
        B, T, D, O, E, R = (4, 256, 512, 512, 8, 16)
        x = jax.random.normal(ks[0], (B, T, D), dtype=jnp.float32)
        language_ids = jax.random.randint(ks[1], (B,), 0, E).astype(jnp.int64)
        W = jax.random.normal(ks[2], (O, D), dtype=jnp.float32) * (1.0 / np.sqrt(D))
        Wr = jax.random.normal(ks[3], (E, D), dtype=jnp.float32) * (1.0 / np.sqrt(D))
        A = jax.random.normal(ks[4], (E, R, D), dtype=jnp.float32) * (1.0 / np.sqrt(D))
        Bm = jax.random.normal(ks[5], (O, R), dtype=jnp.float32) * 0.0
        Bm = jnp.broadcast_to(Bm, (E, O, R)) + jax.random.normal(ks[5], (E, O, R), dtype=jnp.float32) * 0.02
        return {'x': x, 'language_ids': language_ids, 'W': W, 'Wr': Wr, 'A': A, 'B': Bm}
    _L0_cond_all = _L0_cond_setup()
    _L0_cond_in = {k: v for k, v in _L0_cond_all.items() if k in ('W', 'Wr', 'A', 'B')}
    del _L0_cond_all
    return {'x': x, 'itok_B_0_7': itok_B_0_7, 'L0_cond_W': _L0_cond_in['W'], 'L0_cond_Wr': _L0_cond_in['Wr'], 'L0_cond_A': _L0_cond_in['A'], 'L0_cond_B': _L0_cond_in['B']}

def reference(x, itok_B_0_7, L0_cond_W, L0_cond_Wr, L0_cond_A, L0_cond_B):
    import jax
    import jax.numpy as jnp

    def _L0_cond_ref(x, language_ids, W, Wr, A, B):
        import jax, jax.numpy as jnp
        import numpy as np
        TOP_K = 2
        LANG_BIAS = 5.0
        SCALING = 32.0 / 16.0
        LANGUAGE_PAD_ID = -1
        base = jnp.einsum('btd,od->bto', x, W)
        E = Wr.shape[0]
        logits = jnp.einsum('btd,ed->bte', x.astype(jnp.float32), Wr.astype(jnp.float32))
        expert_targets = language_ids
        valid = expert_targets >= 0
        tgt = jnp.where(valid, expert_targets, 0)
        bias = jax.nn.one_hot(tgt, E, dtype=logits.dtype) * LANG_BIAS
        bias = jnp.where(valid[:, None], bias, 0.0)
        logits = logits + bias[:, None, :]
        topw, topi = jax.lax.top_k(logits, TOP_K)
        weights = jax.nn.softmax(topw, axis=-1)
        gates = jnp.sum(jax.nn.one_hot(topi, E, dtype=weights.dtype) * weights[..., None], axis=-2)
        gates = gates.astype(x.dtype)
        h = jnp.einsum('btd,erd->bter', x, A)
        lora_out = jnp.einsum('bter,bte,eor->bto', h, gates, B)
        return base + SCALING * lora_out
    x = x + _L0_cond_ref(x, itok_B_0_7, L0_cond_W, L0_cond_Wr, L0_cond_A, L0_cond_B)
    return x

_drawn_inputs = setup_inputs


def setup_inputs(seed=0):
    import zlib

    import numpy as np

    out = dict(_drawn_inputs(seed))
    spreads = {}
    factors = {'L0_cond_Wr': 5.002}
    for name, (base, spread) in spreads.items():
        noise = np.random.default_rng([zlib.crc32(name.encode()), seed]).standard_normal(out[name].shape)
        drawn = base * np.exp(spread * noise) if base else spread * noise
        out[name] = jnp.asarray(drawn.astype(out[name].dtype))
    for name, factor in factors.items():
        out[name] = (out[name] * factor).astype(out[name].dtype)
    return out
```

```python
import concourse.bass as bass
from concourse import mybir
from contextlib import ExitStack

FP32 = mybir.dt.float32
FP32R = mybir.dt.float32r
BF16 = mybir.dt.bfloat16
I32 = mybir.dt.int32
U32 = mybir.dt.uint32
ALU = mybir.AluOpType
ACT = mybir.ActivationFunctionType

P = 128
SEQS, SEQ_LEN, D = 64, 32, 512
O = 512
E, R = 8, 16
TOKENS = SEQS * SEQ_LEN
TILES = TOKENS // P
KC = D // P
BANK = 512
ER = E * R
BASE = O // 2
REST = O - BASE
HEADS = REST + ER + E
SLOTS = 3
LANG_BIAS = 5.0
SCALING = 2.0
WARM_UP = 8

GROUPS = (TILES - 4) // SLOTS
PEELED = (0, 1)
LAST = (TILES - 2, TILES - 1)
assert PEELED[-1] + 1 + GROUPS * SLOTS == LAST[0]


def cond_resid_program(nc: bass.Bass, xT: bass.AP, x: bass.AP, ids: bass.AP, w_heads: bass.AP,
                       w_base: bass.AP, b: bass.AP, out: bass.AP):
    ctx = ExitStack()
    with ctx:
        def sb(name, shape, dt=FP32):
            return ctx.enter_context(nc.sbuf_tensor(name, shape, dt))

        def ps(name):
            return ctx.enter_context(nc.psum_tensor(name, [P, BANK], FP32))

        def sem(name):
            return ctx.enter_context(nc.semaphore(name))

        xT_sb = sb("xT_sb", [P, TILES, KC * P])
        x_sb = sb("x_sb", [P, TILES, D])
        out_sb = sb("out_sb", [P, TILES, O])
        wh_sb = sb("wh_sb", [P, KC, HEADS])
        wh_hi = sb("wh_hi", [P, KC, HEADS], FP32R)
        wh_lo = sb("wh_lo", [P, KC, HEADS], FP32R)
        wb_sb = sb("wb_sb", [P, KC, BASE])
        wb_hi = sb("wb_hi", [P, KC, BASE], FP32R)
        wb_lo = sb("wb_lo", [P, KC, BASE], FP32R)
        b_sb = sb("b_sb", [ER, O])
        b_hi = sb("b_hi", [ER, O], FP32R)
        b_lo = sb("b_lo", [ER, O], FP32R)
        ids_sb = sb("ids_sb", [P, 1], I32)
        expert = sb("expert", [P, E], I32)
        bias = sb("bias", [P, E])
        ident = sb("ident", [P, P])
        zeros = sb("zeros", [P, BANK], BF16)
        x_hi = [sb(f"x_hi{s}", [P, KC * P], FP32R) for s in range(SLOTS)]
        x_lo = [sb(f"x_lo{s}", [P, KC * P], FP32R) for s in range(SLOTS)]
        gh = [sb(f"gh{s}", [P, ER]) for s in range(SLOTS)]
        ghT_hi = [sb(f"ghT_hi{s}", [ER, P], FP32R) for s in range(SLOTS)]
        ghT_lo = [sb(f"ghT_lo{s}", [ER, P], FP32R) for s in range(SLOTS)]
        logits = sb("logits", [P, E])
        top = sb("top", [P, E])
        top_at = sb("top_at", [P, E], U32)
        top_atf = sb("top_atf", [P, 2])
        e2 = sb("e2", [P, 1])
        den = sb("den", [P, 1])
        rden = sb("rden", [P, 1])
        second = sb("second", [P, E])
        gate = sb("gate", [P, E])

        base_ps = [ps(f"base_ps{s}") for s in range(SLOTS)]
        heads_ps = [ps(f"heads_ps{s}") for s in range(SLOTS)]
        ghT_ps = ps("ghT_ps")
        warm_ps = ps("warm_ps")

        xT_first = [sem(f"xT_first{t}") for t in PEELED]
        x_first = [sem(f"x_first{t}") for t in PEELED]
        xT_group = sem("xT_group")
        x_group = sem("x_group")
        xT_last = sem("xT_last")
        x_last = sem("x_last")
        wh_landed = [sem(f"wh_landed{k}") for k in range(KC)]
        wb_landed = [sem(f"wb_landed{h}") for h in range(2)]
        b_landed = sem("b_landed")
        ids_landed = sem("ids_landed")
        out_stored = sem("out_stored")
        zeros_made = sem("zeros_made")
        ident_zeroed = sem("ident_zeroed")
        ident_made = sem("ident_made")
        expert_made = sem("expert_made")
        bias_made = sem("bias_made")
        wh_hi_made = sem("wh_hi_made")
        wh_lo_made = sem("wh_lo_made")
        wb_hi_made = sem("wb_hi_made")
        wb_lo_made = sem("wb_lo_made")
        b_hi_made = sem("b_hi_made")
        b_lo_made = sem("b_lo_made")
        x_hi_made = sem("x_hi_made")
        x_lo_made = sem("x_lo_made")
        heads_done = sem("heads_done")
        base_done = sem("base_done")
        logits_made = sem("logits_made")
        top_made = sem("top_made")
        top_at_made = sem("top_at_made")
        top_atf_made = sem("top_atf_made")
        e2_made = sem("e2_made")
        den_made = sem("den_made")
        rden_made = sem("rden_made")
        second_made = sem("second_made")
        gate_made = sem("gate_made")
        gh_made = sem("gh_made")
        transposed = sem("transposed")
        ghT_hi_made = sem("ghT_hi_made")
        ghT_lo_made = sem("ghT_lo_made")
        lora_heads_done = sem("lora_heads_done")
        lora_base_done = sem("lora_base_done")
        heads_read = sem("heads_read")
        out_made = sem("out_made")

        block = ctx.enter_context(nc.Block())

        @block.sync
        def _(sp):
            def load(dst, src, t, n, landed):
                sp.dma_start(dst[:, bass.ds(t, n), :], src[:, bass.ds(t, n), :]).then_inc(landed, 16)

            def store(t, n):
                sp.dma_start(out[:, bass.ds(t, n), :], out_sb[:, bass.ds(t, n), :]).then_inc(out_stored, 16)

            load(xT_sb, xT, 0, 1, xT_first[0])
            for k in range(KC):
                sp.dma_start(wh_sb[:, k, :], w_heads[:, k, :]).then_inc(wh_landed[k], 16)
            for h in range(2):
                half = slice(h * KC // 2, (h + 1) * KC // 2)
                sp.dma_start(wb_sb[:, half, :], w_base[:, half, :]).then_inc(wb_landed[h], 16)
            sp.dma_start(ids_sb[:, :], ids.rearrange("(s a) o -> s a o", a=1)
                         .to_broadcast([SEQS, P // SEQS, 1])).then_inc(ids_landed, 16)
            load(xT_sb, xT, 1, 1, xT_first[1])
            sp.dma_start(b_sb[:, :], b).then_inc(b_landed, 16)
            load(xT_sb, xT, 2, SLOTS, xT_group)
            load(x_sb, x, 0, 1, x_first[0])
            load(x_sb, x, 1, 1, x_first[1])
            load(x_sb, x, 2, SLOTS, x_group)
            with sp.Fori(0, GROUPS - 1) as g:
                sp.wait_ge(xT_group, 16 * g + 16)
                sp.wait_ge(x_group, 16 * g + 16)
                load(xT_sb, xT, SLOTS * g + 2 + SLOTS, SLOTS, xT_group)
                load(x_sb, x, SLOTS * g + 2 + SLOTS, SLOTS, x_group)
            load(xT_sb, xT, LAST[0], len(LAST), xT_last)
            load(x_sb, x, LAST[0], len(LAST), x_last)
            sp.wait_ge(out_made, len(PEELED))
            store(0, len(PEELED))
            with sp.Fori(0, GROUPS) as g:
                sp.wait_ge(out_made, SLOTS * g + 2 + SLOTS)
                store(SLOTS * g + 2, SLOTS)
            sp.wait_ge(out_made, TILES - 1)
            store(LAST[0], 1)
            sp.wait_ge(heads_read, TILES)
            sp.dma_start(out[:, TILES - 1, BASE:O], out_sb[:, TILES - 1, BASE:O]).then_inc(out_stored, 16)
            sp.wait_ge(out_made, TILES)
            sp.dma_start(out[:, TILES - 1, 0:BASE], out_sb[:, TILES - 1, 0:BASE]).then_inc(out_stored, 16)
            sp.wait_ge(out_stored, 16 * (GROUPS + 4))

        @block.gpsimd
        def _(pool):
            nc.gpsimd.memset(ident[:, :], 0.0).then_inc(ident_zeroed, 1)
            nc.gpsimd.iota(expert[:, :], pattern=[[1, E]], base=0, channel_multiplier=0).then_inc(expert_made, 1)
            pool.wait_ge(ident_zeroed, 1)
            nc.gpsimd.affine_select(out=ident[:, :], in_=ident[:, :], compare_op=ALU.not_equal, fill=1.0, base=0,
                                    pattern=[[-1, P]], channel_multiplier=1).then_inc(ident_made, 1)

            def x_lower(t, s):
                pool.wait_ge(x_hi_made, t + 1)
                nc.gpsimd.tensor_tensor(x_lo[s][:, :], xT_sb[:, t, :], x_hi[s][:, :].bitcast(FP32),
                                        ALU.subtract).then_inc(x_lo_made, 1)

            for t in PEELED:
                x_lower(t, t % SLOTS)
            with pool.Fori(0, GROUPS) as g:
                for j in range(2, 2 + SLOTS):
                    x_lower(SLOTS * g + j, j % SLOTS)
            for t in LAST:
                x_lower(t, t % SLOTS)

        @block.scalar
        def _(act):
            def x_upper(t, s, landed, count):
                act.wait_ge(landed, count)
                if isinstance(t, int) and t < SLOTS:
                    pass
                else:
                    act.wait_ge(base_done, t - SLOTS + 1)
                nc.scalar.activation(x_hi[s][:, :], xT_sb[:, t, :], ACT.Copy).then_inc(x_hi_made, 1)

            def ghT_upper(t, s):
                act.wait_ge(transposed, t + 1)
                nc.scalar.activation(ghT_hi[s][:, :], ghT_ps[:, 0:P], ACT.Copy).then_inc(ghT_hi_made, 1)

            def exponential(t):
                act.wait_ge(top_made, t + 1)
                nc.scalar.activation(e2[:, :], top[:, 0:1], ACT.Exp, scale=-1.0,
                                     bias=top[:, 1:2]).then_inc(e2_made, 1)

            x_upper(0, 0, xT_first[0], 16)
            for k in range(KC):
                act.wait_ge(wh_landed[k], 16)
                nc.scalar.activation(wh_hi[:, k, :], wh_sb[:, k, :], ACT.Copy).then_inc(wh_hi_made, 1)
            for h in range(2):
                half = slice(h * KC // 2, (h + 1) * KC // 2)
                act.wait_ge(wb_landed[h], 16)
                nc.scalar.activation(wb_hi[:, half, :], wb_sb[:, half, :], ACT.Copy).then_inc(wb_hi_made, 1)
            x_upper(1, 1, xT_first[1], 16)
            exponential(0)
            act.wait_ge(b_landed, 16)
            nc.scalar.activation(b_hi[:, :], b_sb[:, :], ACT.Copy, scale=SCALING).then_inc(b_hi_made, 1)

            def step(t, j, landed, count):
                x_upper(t + 1, (j + 1) % SLOTS, landed, count)
                ghT_upper(t - 1, (j - 1) % SLOTS)
                exponential(t)

            step(1, 1, xT_group, 16)
            with act.Fori(0, GROUPS - 1) as g:
                for j in range(2, 2 + SLOTS):
                    step(SLOTS * g + j, j, xT_group, 16 * g + 16 * (1 + (j == 1 + SLOTS)))
            for j in range(2, 2 + SLOTS):
                end = j == 1 + SLOTS
                step(SLOTS * (GROUPS - 1) + j, j, xT_last if end else xT_group, 16 if end else 16 * GROUPS)
            step(LAST[0], LAST[0], xT_last, 16)
            ghT_upper(LAST[0], LAST[0] % SLOTS)
            exponential(LAST[1])
            ghT_upper(LAST[1], LAST[1] % SLOTS)

        @block.vector
        def _(dve):
            def ghT_lower(t, s):
                dve.wait_ge(ghT_hi_made, t + 1)
                nc.vector.tensor_tensor(ghT_lo[s][:, :], ghT_ps[:, 0:P], ghT_hi[s][:, :].bitcast(FP32),
                                        ALU.subtract).then_inc(ghT_lo_made, 1)

            def best_two(t, s):
                dve.wait_ge(heads_done, t + 1)
                nc.vector.tensor_tensor(logits[:, :], heads_ps[s][:, HEADS - E:HEADS], bias[:, :],
                                        ALU.add).then_inc(logits_made, 1)
                dve.wait_ge(bias_made, 1)
                dve.wait_ge(logits_made, t + 1)
                nc.vector.max(top[:, :], logits[:, :]).then_inc(top_made, 1)
                dve.wait_ge(bias_made, 1)
                dve.wait_ge(top_made, t + 1)
                nc.vector.max_index(top_at[:, :], top[:, :], logits[:, :]).then_inc(top_at_made, 1)
                dve.wait_ge(top_at_made, t + 1)
                nc.vector.tensor_copy(top_atf[:, :], top_at[:, 0:2]).then_inc(top_atf_made, 1)
                dve.wait_ge(e2_made, t + 1)
                nc.vector.tensor_scalar(den[:, :], e2[:, :], 1.0, None, ALU.add).then_inc(den_made, 1)

            def gates(t):
                dve.wait_ge(top_atf_made, t + 1)
                nc.vector.tensor_scalar(second[:, :], expert[:, :], top_atf[:, 1:2], e2[:, :],
                                        ALU.is_equal, ALU.mult).then_inc(second_made, 1)
                dve.wait_ge(den_made, t + 1)
                nc.vector.reciprocal(rden[:, :], den[:, :]).then_inc(rden_made, 1)
                dve.wait_ge(second_made, t + 1)
                nc.vector.scalar_tensor_tensor(gate[:, :], expert[:, :], top_atf[:, 0:1], second[:, :],
                                               ALU.is_equal, ALU.add).then_inc(gate_made, 1)

            def gated(t, s):
                dve.wait_ge(rden_made, t + 1)
                dve.wait_ge(gate_made, t + 1)
                nc.vector.scalar_tensor_tensor(
                    gh[s][:, :].rearrange("p (e r) -> p e r", r=R),
                    heads_ps[s][:, REST:REST + ER].rearrange("p (e r) -> p e r", r=R), rden[:, :],
                    gate[:, :].rearrange("p (e a) -> p e a", a=1).to_broadcast([P, E, R]),
                    ALU.mult, ALU.mult).then_inc(gh_made, 1)

            def out_rest(t, s, landed, count):
                dve.wait_ge(lora_heads_done, t + 1)
                dve.wait_ge(landed, count)
                nc.vector.tensor_tensor(out_sb[:, t, BASE:O], heads_ps[s][:, 0:REST], x_sb[:, t, BASE:O],
                                        ALU.add).then_inc(heads_read, 1)

            def out_base(t, s):
                dve.wait_ge(lora_base_done, t + 1)
                nc.vector.tensor_tensor(out_sb[:, t, 0:BASE], base_ps[s][:, 0:BASE], x_sb[:, t, 0:BASE],
                                        ALU.add).then_inc(out_made, 1)

            def step(t, j, landed, count):
                s, before = j % SLOTS, (j - 1) % SLOTS
                ghT_lower(t - 1, before)
                best_two(t, s)
                gates(t)
                gated(t, s)
                out_rest(t - 1, before, landed, count)
                out_base(t - 1, before)

            nc.vector.memset(zeros[:, :], 0.0).then_inc(zeros_made, 1)
            for k in range(KC):
                dve.wait_ge(wh_hi_made, k + 1)
                nc.vector.tensor_tensor(wh_lo[:, k, :], wh_sb[:, k, :], wh_hi[:, k, :].bitcast(FP32),
                                        ALU.subtract).then_inc(wh_lo_made, 1)
            for h in range(2):
                half = slice(h * KC // 2, (h + 1) * KC // 2)
                dve.wait_ge(wb_hi_made, h + 1)
                nc.vector.tensor_tensor(wb_lo[:, half, :], wb_sb[:, half, :], wb_hi[:, half, :].bitcast(FP32),
                                        ALU.subtract).then_inc(wb_lo_made, 1)
            dve.wait_ge(expert_made, 1)
            dve.wait_ge(ids_landed, 16)
            nc.vector.tensor_scalar(bias[:, :], expert[:, :], ids_sb[:, :], LANG_BIAS, ALU.is_equal,
                                    ALU.mult).then_inc(bias_made, 1)
            dve.wait_ge(bias_made, 1)
            best_two(0, 0)
            gates(0)
            gated(0, 0)
            dve.wait_ge(b_hi_made, 1)
            nc.vector.scalar_tensor_tensor(b_lo[:, :], b_sb[:, :], SCALING, b_hi[:, :].bitcast(FP32), ALU.mult,
                                           ALU.subtract).then_inc(b_lo_made, 1)
            step(1, 1, x_first[0], 16)
            step(2, 2, x_first[1], 16)
            with dve.Fori(0, GROUPS) as g:
                for j in range(3, 3 + SLOTS):
                    step(SLOTS * g + j, j, x_group, 16 * g + 16)
            step(LAST[1], LAST[1], x_last, 16)
            ghT_lower(LAST[1], LAST[1] % SLOTS)
            out_rest(LAST[1], LAST[1] % SLOTS, x_last, 16)
            out_base(LAST[1], LAST[1] % SLOTS)

        @block.tensor
        def _(pe):
            def project(dst, xs_s, parts, k):
                hi, lo = parts
                for n, (xs, ws) in enumerate(((x_hi, hi), (x_hi, lo), (x_lo, hi))):
                    last = nc.tensor.matmul(dst, xs[xs_s][:, k * P:(k + 1) * P], ws[:, k, :],
                                            start=(k == 0 and n == 0), stop=(k == KC - 1 and n == 2))
                return last

            def heads(s, chunks):
                for k in chunks:
                    last = project(heads_ps[s][:, 0:HEADS], s, (wh_hi, wh_lo), k)
                return last

            def base(s, chunks):
                for k in chunks:
                    last = project(base_ps[s][:, 0:BASE], s, (wb_hi, wb_lo), k)
                return last

            def transpose(t, s):
                pe.wait_ge(gh_made, t + 1)
                nc.tensor.transpose(ghT_ps[:, 0:P], gh[s][:, :], ident[:, :]).then_inc(transposed, 1)

            def lora(t, s):
                pe.wait_ge(ghT_lo_made, t + 1)
                for dst, cols, done in ((heads_ps[s][:, 0:REST], slice(BASE, O), lora_heads_done),
                                        (base_ps[s][:, 0:BASE], slice(0, BASE), lora_base_done)):
                    for n, (gs, bs) in enumerate(((ghT_hi, b_hi), (ghT_hi, b_lo), (ghT_lo, b_hi))):
                        last = nc.tensor.matmul(dst, gs[s][:, :], bs[:, cols], start=False, stop=(n == 2),
                                                skip_group_check=True)
                    last.then_inc(done, 1)

            def step(t, j):
                s, before = j % SLOTS, (j - 1) % SLOTS
                pe.wait_ge(x_hi_made, t + 1)
                pe.wait_ge(x_lo_made, t + 1)
                if not (isinstance(t, int) and t < SLOTS):
                    pe.wait_ge(out_made, t - SLOTS + 1)
                heads(s, (0, 1, 2))
                transpose(t - 1, before)
                heads(s, (3,)).then_inc(heads_done, 1)
                base(s, (0, 1, 2))
                lora(t - 1, before)
                base(s, (3,)).then_inc(base_done, 1)

            pe.wait_ge(zeros_made, 1)
            for _ in range(WARM_UP):
                nc.tensor.matmul(warm_ps[:, :], zeros[:, 0:P], zeros[:, :], start=True, stop=True)
            pe.wait_ge(x_hi_made, 1)
            for k in range(KC):
                for n, (xs, ws) in enumerate(((x_hi, wh_hi), (x_hi, wh_lo), (x_lo, wh_hi))):
                    if n == 0:
                        pe.wait_ge(wh_hi_made, k + 1)
                    if n == 1:
                        pe.wait_ge(wh_lo_made, k + 1)
                    if n == 2 and k == 0:
                        pe.wait_ge(x_lo_made, 1)
                    last = nc.tensor.matmul(heads_ps[0][:, 0:HEADS], xs[0][:, k * P:(k + 1) * P], ws[:, k, :],
                                            start=(k == 0 and n == 0), stop=(k == KC - 1 and n == 2))
            last.then_inc(heads_done, 1)
            for h in range(2):
                pe.wait_ge(wb_hi_made, h + 1)
                pe.wait_ge(wb_lo_made, h + 1)
                last = base(0, range(h * KC // 2, (h + 1) * KC // 2))
            last.then_inc(base_done, 1)
            pe.wait_ge(ident_made, 1)
            pe.wait_ge(b_lo_made, 1)
            step(1, 1)
            with pe.Fori(0, GROUPS) as g:
                for j in range(2, 2 + SLOTS):
                    step(SLOTS * g + j, j)
            for t in LAST:
                step(t, t)
            transpose(LAST[1], LAST[1] % SLOTS)
            lora(LAST[1], LAST[1] % SLOTS)


def kernel(x, itok_B_0_7, L0_cond_W, L0_cond_Wr, L0_cond_A, L0_cond_B):
    import numpy as np
    import concourse.bacc as bacc
    from concourse.bass_utils import run_bass_kernel_spmd

    x, W, Wr, A, B = (np.asarray(a) for a in (x, L0_cond_W, L0_cond_Wr, L0_cond_A, L0_cond_B))
    tokens = x.reshape(P, TILES, KC, P)
    heads = np.concatenate([W[BASE:], A.reshape(ER, D), Wr]).reshape(HEADS, KC, P)
    arrays = {
        "in_xT": np.ascontiguousarray(tokens.transpose(3, 1, 2, 0)).reshape(P, TILES, KC * P),
        "in_x": np.ascontiguousarray(tokens).reshape(P, TILES, D),
        "in_ids": np.ascontiguousarray(np.asarray(itok_B_0_7).reshape(SEQS, 1)),
        "in_w_heads": np.ascontiguousarray(heads.transpose(2, 1, 0)),
        "in_w_base": np.ascontiguousarray(W[:BASE].reshape(BASE, KC, P).transpose(2, 1, 0)),
        "in_b": np.ascontiguousarray(B.transpose(0, 2, 1)).reshape(ER, O),
    }
    nc = bacc.Bacc("TRN2", target_bir_lowering=False, num_devices=1)
    args = [nc.dram_tensor(name, a.shape, mybir.dt.from_np(a.dtype), kind="ExternalInput").ap()
            for name, a in arrays.items()]
    args.append(nc.dram_tensor("out", (P, TILES, O), FP32, kind="ExternalOutput").ap())
    cond_resid_program(nc, *args)
    r = run_bass_kernel_spmd(nc, [arrays], core_ids=[0])
    return r.results[0]["out"].reshape(SEQS, SEQ_LEN, O)
```

```python
import concourse.bass as bass
from concourse import mybir
from contextlib import ExitStack

FP32 = mybir.dt.float32
FP32R = mybir.dt.float32r
BF16 = mybir.dt.bfloat16
I32 = mybir.dt.int32
U32 = mybir.dt.uint32
ALU = mybir.AluOpType
ACT = mybir.ActivationFunctionType

P = 128
SEQS, SEQ_LEN, D = 64, 32, 512
O = 512
E, R = 8, 16
TOKENS = SEQS * SEQ_LEN
TILES = TOKENS // P
KC = D // P
BANK = 512
ER = E * R
BASE = O // 2
REST = O - BASE
HEADS = REST + ER + E
SLOTS = 3
LANG_BIAS = 5.0
SCALING = 2.0
WARM_UP = 8

PEELED = (0, 1)
HALVES = (slice(0, D // 2), slice(D // 2, D))
GROUPS = 4
GROUPED = GROUPS * SLOTS


def cond_resid_program(nc: bass.Bass, xT: bass.AP, x: bass.AP, ids: bass.AP, w_heads: bass.AP,
                       w_base: bass.AP, b: bass.AP, out: bass.AP):
    ctx = ExitStack()
    with ctx:
        def sb(name, shape, dt=FP32):
            return ctx.enter_context(nc.sbuf_tensor(name, shape, dt))

        def ps(name):
            return ctx.enter_context(nc.psum_tensor(name, [P, BANK], FP32))

        def sem(name):
            return ctx.enter_context(nc.semaphore(name))

        xT_sb = sb("xT_sb", [P, TILES, KC * P])
        x_sb = sb("x_sb", [P, TILES, D])
        out_sb = sb("out_sb", [P, TILES, O])
        wh_sb = sb("wh_sb", [P, KC, HEADS])
        wh_hi = sb("wh_hi", [P, KC, HEADS], FP32R)
        wh_lo = sb("wh_lo", [P, KC, HEADS], FP32R)
        wb_sb = sb("wb_sb", [P, KC, BASE])
        wb_hi = sb("wb_hi", [P, KC, BASE], FP32R)
        wb_lo = sb("wb_lo", [P, KC, BASE], FP32R)
        b_sb = sb("b_sb", [ER, O])
        b_hi = sb("b_hi", [ER, O], FP32R)
        b_lo = sb("b_lo", [ER, O], FP32R)
        ids_sb = sb("ids_sb", [P, 1], I32)
        expert = sb("expert", [P, E], I32)
        bias = sb("bias", [P, E])
        ident = sb("ident", [P, P])
        zeros = sb("zeros", [P, P // 2])
        x_hi = [sb(f"x_hi{s}", [P, KC * P], FP32R) for s in range(SLOTS)]
        x_lo = [sb(f"x_lo{s}", [P, KC * P], FP32R) for s in range(SLOTS)]
        gh = [sb(f"gh{s}", [P, ER]) for s in range(SLOTS)]
        ghT_hi = [sb(f"ghT_hi{s}", [ER, P], FP32R) for s in range(SLOTS)]
        ghT_lo = [sb(f"ghT_lo{s}", [ER, P], FP32R) for s in range(SLOTS)]
        logits = sb("logits", [P, E])
        top = sb("top", [P, E])
        top_at = sb("top_at", [P, E], U32)
        top_atf = sb("top_atf", [P, 2])
        e2 = sb("e2", [P, 1])
        den = sb("den", [P, 1])
        rden = sb("rden", [P, 1])
        second = sb("second", [P, E])
        gate = sb("gate", [P, E])

        base_ps = [ps(f"base_ps{s}") for s in range(SLOTS)]
        heads_ps = [ps(f"heads_ps{s}") for s in range(SLOTS)]
        ghT_ps = ps("ghT_ps")
        warm_ps = ps("warm_ps")

        xT_first = [[sem(f"xT_first{t}_{h}") for h in range(2)] for t in PEELED]
        xT_third = sem("xT_third")
        xT_group = sem("xT_group")
        x_group = sem("x_group")
        xT_last = sem("xT_last")
        x_last = sem("x_last")
        wh_landed = [sem(f"wh_landed{k}") for k in range(KC)]
        wb_landed = [sem(f"wb_landed{k}") for k in range(KC)]
        b_landed = sem("b_landed")
        ids_landed = sem("ids_landed")
        out_stored = sem("out_stored")
        zeros_made = sem("zeros_made")
        ident_zeroed = sem("ident_zeroed")
        ident_made = sem("ident_made")
        expert_made = sem("expert_made")
        bias_made = sem("bias_made")
        wh_hi_made = sem("wh_hi_made")
        wh_lo_made = sem("wh_lo_made")
        wb_hi_made = sem("wb_hi_made")
        wb_lo_made = sem("wb_lo_made")
        b_hi_made = sem("b_hi_made")
        b_lo_made = sem("b_lo_made")
        half_hi_made = sem("half_hi_made")
        half_lo_made = sem("half_lo_made")
        x_hi_made = sem("x_hi_made")
        x_lo_made = sem("x_lo_made")
        heads_done = sem("heads_done")
        base_done = sem("base_done")
        logits_made = sem("logits_made")
        top_made = sem("top_made")
        top_at_made = sem("top_at_made")
        top_atf_made = sem("top_atf_made")
        e2_made = sem("e2_made")
        den_made = sem("den_made")
        rden_made = sem("rden_made")
        second_made = sem("second_made")
        gate_made = sem("gate_made")
        gh_made = sem("gh_made")
        transposed = sem("transposed")
        ghT_hi_made = sem("ghT_hi_made")
        ghT_lo_made = sem("ghT_lo_made")
        lora_heads_done = sem("lora_heads_done")
        lora_base_done = sem("lora_base_done")
        heads_read = sem("heads_read")
        out_made = sem("out_made")

        block = ctx.enter_context(nc.Block())

        @block.sync
        def _(sp):
            def load(dst, src, t, n, landed):
                sp.dma_start(dst[:, bass.ds(t, n), :], src[:, bass.ds(t, n), :]).then_inc(landed, 16)

            def store(t, n):
                sp.dma_start(out[:, bass.ds(t, n), :], out_sb[:, bass.ds(t, n), :]).then_inc(out_stored, 16)

            def load_half(t, h):
                sp.dma_start(xT_sb[:, t, HALVES[h]], xT[:, t, HALVES[h]]).then_inc(xT_first[t][h], 16)

            load_half(0, 0)
            for k in range(KC):
                sp.dma_start(wh_sb[:, k, :], w_heads[:, k, :]).then_inc(wh_landed[k], 16)
                if k == 0:
                    load_half(0, 1)
            for k in range(KC):
                sp.dma_start(wb_sb[:, k, :], w_base[:, k, :]).then_inc(wb_landed[k], 16)
            load_half(1, 0)
            load_half(1, 1)
            load(xT_sb, xT, 2, 1, xT_third)
            sp.dma_start(ids_sb[:, :], ids.rearrange("(s a) o -> s a o", a=1)
                         .to_broadcast([SEQS, P // SEQS, 1])).then_inc(ids_landed, 16)
            sp.dma_start(b_sb[:, :], b).then_inc(b_landed, 16)
            load(xT_sb, xT, 3, SLOTS, xT_group)
            load(x_sb, x, 0, SLOTS, x_group)
            with sp.Fori(0, GROUPS - 2) as g:
                sp.wait_ge(xT_group, 16 * g + 16)
                sp.wait_ge(x_group, 16 * g + 16)
                load(xT_sb, xT, SLOTS * g + 3 + SLOTS, SLOTS, xT_group)
                load(x_sb, x, SLOTS * g + SLOTS, SLOTS, x_group)
            sp.wait_ge(x_group, 16 * (GROUPS - 1))
            load(x_sb, x, GROUPED - SLOTS, SLOTS, x_group)
            load(xT_sb, xT, GROUPED, TILES - GROUPED, xT_last)
            load(x_sb, x, GROUPED, TILES - GROUPED, x_last)
            with sp.Fori(0, GROUPS) as g:
                sp.wait_ge(out_made, SLOTS * g + SLOTS)
                store(SLOTS * g, SLOTS)
            for t in range(GROUPED, TILES - 1):
                sp.wait_ge(out_made, t + 1)
                store(t, 1)
            sp.wait_ge(heads_read, TILES)
            sp.dma_start(out[:, TILES - 1, BASE:O], out_sb[:, TILES - 1, BASE:O]).then_inc(out_stored, 16)
            sp.wait_ge(out_made, TILES)
            sp.dma_start(out[:, TILES - 1, 0:BASE], out_sb[:, TILES - 1, 0:BASE]).then_inc(out_stored, 16)
            sp.wait_ge(out_stored, 16 * (GROUPS + TILES - 1 - GROUPED + 2))

        @block.gpsimd
        def _(pool):
            nc.gpsimd.memset(zeros[:, :], 0.0).then_inc(zeros_made, 1)
            nc.gpsimd.memset(ident[:, :], 0.0).then_inc(ident_zeroed, 1)
            nc.gpsimd.iota(expert[:, :], pattern=[[1, E]], base=0, channel_multiplier=0).then_inc(expert_made, 1)
            pool.wait_ge(ident_zeroed, 1)
            nc.gpsimd.affine_select(out=ident[:, :], in_=ident[:, :], compare_op=ALU.not_equal, fill=1.0, base=0,
                                    pattern=[[-1, P]], channel_multiplier=1).then_inc(ident_made, 1)

            def x_lower(t, s):
                pool.wait_ge(x_hi_made, t - 1)
                nc.gpsimd.tensor_tensor(x_lo[s][:, :], xT_sb[:, t, :], x_hi[s][:, :].bitcast(FP32),
                                        ALU.subtract).then_inc(x_lo_made, 1)

            for t in PEELED:
                for h, half in enumerate(HALVES):
                    pool.wait_ge(half_hi_made, 2 * t + h + 1)
                    nc.gpsimd.tensor_tensor(x_lo[t][:, half], xT_sb[:, t, half], x_hi[t][:, half].bitcast(FP32),
                                            ALU.subtract).then_inc(half_lo_made, 1)
            with pool.Fori(0, GROUPS) as g:
                for j in range(2, 2 + SLOTS):
                    x_lower(SLOTS * g + j, j % SLOTS)
            for t in range(2 + GROUPED, TILES):
                x_lower(t, t % SLOTS)

        @block.scalar
        def _(act):
            def half_upper(t, h):
                act.wait_ge(xT_first[t][h], 16)
                nc.scalar.activation(x_hi[t][:, HALVES[h]], xT_sb[:, t, HALVES[h]],
                                     ACT.Copy).then_inc(half_hi_made, 1)

            def x_upper(t, s, landed, count):
                act.wait_ge(landed, count)
                if not (isinstance(t, int) and t < SLOTS):
                    act.wait_ge(base_done, t - SLOTS + 1)
                nc.scalar.activation(x_hi[s][:, :], xT_sb[:, t, :], ACT.Copy).then_inc(x_hi_made, 1)

            def ghT_upper(t, s):
                act.wait_ge(transposed, t + 1)
                nc.scalar.activation(ghT_hi[s][:, :], ghT_ps[:, 0:P], ACT.Copy).then_inc(ghT_hi_made, 1)

            def exponential(t):
                act.wait_ge(top_made, t + 1)
                nc.scalar.activation(e2[:, :], top[:, 0:1], ACT.Exp, scale=-1.0,
                                     bias=top[:, 1:2]).then_inc(e2_made, 1)

            half_upper(0, 0)
            for k in range(KC):
                act.wait_ge(wh_landed[k], 16)
                nc.scalar.activation(wh_hi[:, k, :], wh_sb[:, k, :], ACT.Copy).then_inc(wh_hi_made, 1)
                if k == 0:
                    half_upper(0, 1)
            for k in range(KC):
                act.wait_ge(wb_landed[k], 16)
                nc.scalar.activation(wb_hi[:, k, :], wb_sb[:, k, :], ACT.Copy).then_inc(wb_hi_made, 1)
            half_upper(1, 0)
            half_upper(1, 1)
            exponential(0)
            act.wait_ge(b_landed, 16)
            nc.scalar.activation(b_hi[:, :], b_sb[:, :], ACT.Copy, scale=SCALING).then_inc(b_hi_made, 1)

            def step(t, j, landed, count):
                x_upper(t + 1, (j + 1) % SLOTS, landed, count)
                ghT_upper(t - 1, (j - 1) % SLOTS)
                exponential(t)

            step(1, 1, xT_third, 16)
            with act.Fori(0, GROUPS - 1) as g:
                for j in range(2, 2 + SLOTS):
                    step(SLOTS * g + j, j, xT_group, 16 * g + 16)
            for t in range(GROUPED - 1, TILES - 1):
                step(t, t, xT_last, 16)
            exponential(TILES - 1)
            ghT_upper(TILES - 2, (TILES - 2) % SLOTS)
            ghT_upper(TILES - 1, (TILES - 1) % SLOTS)

        @block.vector
        def _(dve):
            def ghT_lower(t, s):
                dve.wait_ge(ghT_hi_made, t + 1)
                nc.vector.tensor_tensor(ghT_lo[s][:, :], ghT_ps[:, 0:P], ghT_hi[s][:, :].bitcast(FP32),
                                        ALU.subtract).then_inc(ghT_lo_made, 1)

            def best_two(t, s):
                dve.wait_ge(heads_done, t + 1)
                nc.vector.tensor_tensor(logits[:, :], heads_ps[s][:, HEADS - E:HEADS], bias[:, :],
                                        ALU.add).then_inc(logits_made, 1)
                dve.wait_ge(bias_made, 1)
                dve.wait_ge(logits_made, t + 1)
                nc.vector.max(top[:, :], logits[:, :]).then_inc(top_made, 1)
                dve.wait_ge(bias_made, 1)
                dve.wait_ge(top_made, t + 1)
                nc.vector.max_index(top_at[:, :], top[:, :], logits[:, :]).then_inc(top_at_made, 1)
                dve.wait_ge(top_at_made, t + 1)
                nc.vector.tensor_copy(top_atf[:, :], top_at[:, 0:2]).then_inc(top_atf_made, 1)
                dve.wait_ge(e2_made, t + 1)
                nc.vector.tensor_scalar(den[:, :], e2[:, :], 1.0, None, ALU.add).then_inc(den_made, 1)

            def gates(t):
                dve.wait_ge(top_atf_made, t + 1)
                nc.vector.tensor_scalar(second[:, :], expert[:, :], top_atf[:, 1:2], e2[:, :],
                                        ALU.is_equal, ALU.mult).then_inc(second_made, 1)
                dve.wait_ge(den_made, t + 1)
                nc.vector.reciprocal(rden[:, :], den[:, :]).then_inc(rden_made, 1)
                dve.wait_ge(second_made, t + 1)
                nc.vector.scalar_tensor_tensor(gate[:, :], expert[:, :], top_atf[:, 0:1], second[:, :],
                                               ALU.is_equal, ALU.add).then_inc(gate_made, 1)

            def gated(t, s):
                dve.wait_ge(rden_made, t + 1)
                dve.wait_ge(gate_made, t + 1)
                nc.vector.scalar_tensor_tensor(
                    gh[s][:, :].rearrange("p (e r) -> p e r", r=R),
                    heads_ps[s][:, REST:REST + ER].rearrange("p (e r) -> p e r", r=R), rden[:, :],
                    gate[:, :].rearrange("p (e a) -> p e a", a=1).to_broadcast([P, E, R]),
                    ALU.mult, ALU.mult).then_inc(gh_made, 1)

            def out_rest(t, s, landed, count):
                dve.wait_ge(lora_heads_done, t + 1)
                dve.wait_ge(landed, count)
                nc.vector.tensor_tensor(out_sb[:, t, BASE:O], heads_ps[s][:, 0:REST], x_sb[:, t, BASE:O],
                                        ALU.add).then_inc(heads_read, 1)

            def out_base(t, s):
                dve.wait_ge(lora_base_done, t + 1)
                nc.vector.tensor_tensor(out_sb[:, t, 0:BASE], base_ps[s][:, 0:BASE], x_sb[:, t, 0:BASE],
                                        ALU.add).then_inc(out_made, 1)

            def step(t, j, landed, count):
                s, before = j % SLOTS, (j - 1) % SLOTS
                ghT_lower(t - 1, before)
                best_two(t, s)
                gates(t)
                gated(t, s)
                out_rest(t - 1, before, landed, count)
                out_base(t - 1, before)

            for k in range(KC):
                dve.wait_ge(wh_hi_made, k + 1)
                nc.vector.tensor_tensor(wh_lo[:, k, :], wh_sb[:, k, :], wh_hi[:, k, :].bitcast(FP32),
                                        ALU.subtract).then_inc(wh_lo_made, 1)
            for k in range(KC):
                dve.wait_ge(wb_hi_made, k + 1)
                nc.vector.tensor_tensor(wb_lo[:, k, :], wb_sb[:, k, :], wb_hi[:, k, :].bitcast(FP32),
                                        ALU.subtract).then_inc(wb_lo_made, 1)
            dve.wait_ge(expert_made, 1)
            dve.wait_ge(ids_landed, 16)
            nc.vector.tensor_scalar(bias[:, :], expert[:, :], ids_sb[:, :], LANG_BIAS, ALU.is_equal,
                                    ALU.mult).then_inc(bias_made, 1)
            dve.wait_ge(bias_made, 1)
            best_two(0, 0)
            gates(0)
            gated(0, 0)
            dve.wait_ge(b_hi_made, 1)
            nc.vector.scalar_tensor_tensor(b_lo[:, :], b_sb[:, :], SCALING, b_hi[:, :].bitcast(FP32), ALU.mult,
                                           ALU.subtract).then_inc(b_lo_made, 1)
            with dve.Fori(0, GROUPS) as g:
                for j in range(1, 1 + SLOTS):
                    step(SLOTS * g + j, j, x_group, 16 * g + 16)
            for t in range(GROUPED + 1, TILES - 2):
                step(t, t, x_last, 16)
            t0, t1, t2 = range(TILES - 3, TILES)
            s0, s1, s2 = t0 % SLOTS, t1 % SLOTS, t2 % SLOTS
            ghT_lower(t0, s0)
            best_two(t1, s1)
            gates(t1)
            gated(t1, s1)
            out_rest(t0, s0, x_last, 16)
            out_base(t0, s0)
            best_two(t2, s2)
            gates(t2)
            ghT_lower(t1, s1)
            gated(t2, s2)
            out_rest(t1, s1, x_last, 16)
            out_base(t1, s1)
            ghT_lower(t2, s2)
            out_rest(t2, s2, x_last, 16)
            out_base(t2, s2)

        @block.tensor
        def _(pe):
            def product(dst, s, ws, k, n):
                xs = x_lo if n == 2 else x_hi
                return nc.tensor.matmul(dst, xs[s][:, k * P:(k + 1) * P], ws[n % 2][:, k, :],
                                        start=(k == 0 and n == 0), stop=(k == KC - 1 and n == 2))

            def heads(s, chunks):
                for k in chunks:
                    for n in range(3):
                        last = product(heads_ps[s][:, 0:HEADS], s, (wh_hi, wh_lo), k, n)
                return last

            def base(s, chunks):
                for k in chunks:
                    for n in range(3):
                        last = product(base_ps[s][:, 0:BASE], s, (wb_hi, wb_lo), k, n)
                return last

            def transpose(t, s):
                pe.wait_ge(gh_made, t + 1)
                nc.tensor.transpose(ghT_ps[:, 0:P], gh[s][:, :], ident[:, :]).then_inc(transposed, 1)

            def lora(t, s):
                halves = ((heads_ps[s][:, 0:REST], slice(BASE, O), lora_heads_done),
                          (base_ps[s][:, 0:BASE], slice(0, BASE), lora_base_done))
                pe.wait_ge(ghT_hi_made, t + 1)
                for bs in (b_hi, b_lo):
                    for dst, cols, _ in halves:
                        nc.tensor.matmul(dst, ghT_hi[s][:, :], bs[:, cols], start=False, stop=False,
                                         skip_group_check=True)
                pe.wait_ge(ghT_lo_made, t + 1)
                for dst, cols, done in halves:
                    nc.tensor.matmul(dst, ghT_lo[s][:, :], b_hi[:, cols], start=False, stop=True,
                                     skip_group_check=True).then_inc(done, 1)

            def tile_ready(t):
                pe.wait_ge(x_hi_made, t - 1)
                pe.wait_ge(x_lo_made, t - 1)
                if not (isinstance(t, int) and t < SLOTS):
                    pe.wait_ge(out_made, t - SLOTS + 1)

            def step(t, j):
                s, before = j % SLOTS, (j - 1) % SLOTS
                tile_ready(t)
                heads(s, (0, 1, 2))
                transpose(t - 1, before)
                heads(s, (3,)).then_inc(heads_done, 1)
                base(s, (0, 1, 2))
                lora(t - 1, before)
                base(s, (3,)).then_inc(base_done, 1)

            pe.wait_ge(zeros_made, 1)
            zero_columns = zeros[:, :].bitcast(BF16)
            for _ in range(WARM_UP):
                nc.tensor.matmul(warm_ps[:, :], zero_columns,
                                 zero_columns.rearrange("p (a c) -> p a c", a=1).to_broadcast([P, BANK // P, P]),
                                 start=True, stop=True)
            for k in range(KC):
                half = k // (KC // 2)
                pe.wait_ge(half_hi_made, half + 1)
                pe.wait_ge(wh_hi_made, k + 1)
                product(heads_ps[0][:, 0:HEADS], 0, (wh_hi, wh_lo), k, 0)
                pe.wait_ge(wh_lo_made, k + 1)
                product(heads_ps[0][:, 0:HEADS], 0, (wh_hi, wh_lo), k, 1)
                pe.wait_ge(half_lo_made, half + 1)
                last = product(heads_ps[0][:, 0:HEADS], 0, (wh_hi, wh_lo), k, 2)
            last.then_inc(heads_done, 1)
            for k in range(KC):
                pe.wait_ge(wb_hi_made, k + 1)
                pe.wait_ge(wb_lo_made, k + 1)
                last = base(0, (k,))
            last.then_inc(base_done, 1)
            pe.wait_ge(half_hi_made, 3)
            pe.wait_ge(half_lo_made, 3)
            heads(1, (0, 1))
            pe.wait_ge(half_hi_made, 4)
            pe.wait_ge(half_lo_made, 4)
            heads(1, (2, 3)).then_inc(heads_done, 1)
            base(1, (0, 1))
            pe.wait_ge(ident_made, 1)
            transpose(0, 0)
            base(1, (2, 3)).then_inc(base_done, 1)
            pe.wait_ge(b_lo_made, 1)
            lora(0, 0)
            step(2, 2)
            with pe.Fori(0, GROUPS - 1) as g:
                for j in range(3, 3 + SLOTS):
                    step(SLOTS * g + j, j)
            for t in range(GROUPED, TILES - 2):
                step(t, t)
            t0, t1, t2 = range(TILES - 3, TILES)
            s0, s1, s2 = t0 % SLOTS, t1 % SLOTS, t2 % SLOTS
            tile_ready(t1)
            heads(s1, (0, 1, 2))
            transpose(t0, s0)
            heads(s1, (3,)).then_inc(heads_done, 1)
            tile_ready(t2)
            heads(s2, (0, 1))
            lora(t0, s0)
            heads(s2, (2, 3)).then_inc(heads_done, 1)
            base(s1, range(KC)).then_inc(base_done, 1)
            transpose(t1, s1)
            base(s2, (0, 1))
            lora(t1, s1)
            base(s2, (2,))
            transpose(t2, s2)
            base(s2, (3,)).then_inc(base_done, 1)
            lora(t2, s2)


def kernel(x, itok_B_0_7, L0_cond_W, L0_cond_Wr, L0_cond_A, L0_cond_B):
    import numpy as np
    import concourse.bacc as bacc
    from concourse.bass_utils import run_bass_kernel_spmd

    x, W, Wr, A, B = (np.asarray(a) for a in (x, L0_cond_W, L0_cond_Wr, L0_cond_A, L0_cond_B))
    tokens = x.reshape(P, TILES, KC, P)
    heads = np.concatenate([W[BASE:], A.reshape(ER, D), Wr]).reshape(HEADS, KC, P)
    arrays = {
        "in_xT": np.ascontiguousarray(tokens.transpose(3, 1, 2, 0)).reshape(P, TILES, KC * P),
        "in_x": np.ascontiguousarray(tokens).reshape(P, TILES, D),
        "in_ids": np.ascontiguousarray(np.asarray(itok_B_0_7).reshape(SEQS, 1)),
        "in_w_heads": np.ascontiguousarray(heads.transpose(2, 1, 0)),
        "in_w_base": np.ascontiguousarray(W[:BASE].reshape(BASE, KC, P).transpose(2, 1, 0)),
        "in_b": np.ascontiguousarray(B.transpose(0, 2, 1)).reshape(ER, O),
    }
    nc = bacc.Bacc("TRN2", target_bir_lowering=False, num_devices=1)
    args = [nc.dram_tensor(name, a.shape, mybir.dt.from_np(a.dtype), kind="ExternalInput").ap()
            for name, a in arrays.items()]
    args.append(nc.dram_tensor("out", (P, TILES, O), FP32, kind="ExternalOutput").ap())
    cond_resid_program(nc, *args)
    r = run_bass_kernel_spmd(nc, [arrays], core_ids=[0])
    return r.results[0]["out"].reshape(SEQS, SEQ_LEN, O)
```
